# Optimizing a Trainium2 kernel written in Bass

```python
import numpy as np
import jax
import jax.numpy as jnp

def _softmax(x, axis=-1):
    return jax.nn.softmax(x, axis=axis)

def _gelu(x):
    return jax.nn.gelu(x, approximate=True)

def _silu(x):
    return jax.nn.silu(x)

def _sigmoid(x):
    return jax.nn.sigmoid(x)

def _layernorm(x, axis=-1, eps=1e-05):
    m = jnp.mean(x, axis=axis, keepdims=True)
    v = jnp.var(x, axis=axis, keepdims=True)
    return (x - m) / jnp.sqrt(v + eps)

def _scatter_add(tgt, idx, src, axis=0):
    return tgt.at[idx].add(src)

def _segment_sum(src, seg, n):
    return jax.ops.segment_sum(src, seg, n)
kernel_name = 'mk_rec_standalone_d1_rec_r8_bad525'

def setup_inputs(seed: int=0):
    np.random.seed(seed)
    _w = jnp.asarray

    def _rec_inputs():
        import jax
        import jax.numpy as jnp
        _rk = jax.random.key(seed)
        r_feat_emb = -0.000292821 + 1.00034 * jax.random.normal(jax.random.fold_in(_rk, 1), (2048, 32, 64), jnp.float32)
        return r_feat_emb
    r_feat_emb = _rec_inputs()

    def _L0_rec_setup():
        import jax, jax.numpy as jnp
        import numpy as np
        EMB_DIM = 64
        NUM_FIELDS = 32
        NUM_PAIRS = NUM_FIELDS * (NUM_FIELDS - 1) // 2
        D1 = 256
        BATCH = 256
        key = jax.random.key(seed)
        k1, k2, k3 = jax.random.split(key, 3)
        feat_emb = jax.random.normal(k1, (BATCH, NUM_FIELDS, EMB_DIM), dtype=jnp.float32)
        lim_k = float(np.sqrt(6.0 / (EMB_DIM + EMB_DIM)))
        kernel = jax.random.uniform(k2, (EMB_DIM, NUM_PAIRS, EMB_DIM), minval=-lim_k, maxval=lim_k, dtype=jnp.float32)
        lim_w = float(np.sqrt(6.0 / (NUM_PAIRS + D1)))
        W = jax.random.uniform(k3, (D1, NUM_PAIRS), minval=-lim_w, maxval=lim_w, dtype=jnp.float32)
        b = jnp.zeros((D1,), dtype=jnp.float32)
        return {'feat_emb': feat_emb, 'kernel': kernel, 'W': W, 'b': b}
    _L0_rec_all = _L0_rec_setup()
    _L0_rec_in = {k: v for k, v in _L0_rec_all.items() if k in ('kernel', 'W', 'b')}
    del _L0_rec_all
    return {'r_feat_emb': r_feat_emb, 'L0_rec_kernel': _L0_rec_in['kernel'], 'L0_rec_W': _L0_rec_in['W'], 'L0_rec_b': _L0_rec_in['b']}

def reference(r_feat_emb, L0_rec_kernel, L0_rec_W, L0_rec_b):
    import jax
    import jax.numpy as jnp

    def _L0_rec_ref(feat_emb, kernel, W, b):
        import jax, jax.numpy as jnp
        import numpy as np
        EMB_DIM = 64
        NUM_FIELDS = 32
        NUM_PAIRS = NUM_FIELDS * (NUM_FIELDS - 1) // 2
        D1 = 256
        BATCH = 256
        num_fields = feat_emb.shape[1]
        rows, cols = np.triu_indices(num_fields, k=1)
        p = feat_emb[:, rows, :]
        q = feat_emb[:, cols, :]
        pij = jnp.einsum('bpe,dpe,bpd->bp', p, kernel, q)
        return pij @ W.T + b
    y = _L0_rec_ref(r_feat_emb, L0_rec_kernel, L0_rec_W, L0_rec_b)
    return y

_drawn_inputs = setup_inputs


def setup_inputs(seed=0):
    import zlib

    import numpy as np

    out = dict(_drawn_inputs(seed))
    spreads = {'L0_rec_b': (0.0, 0.728)}
    factors = {}
    for name, (base, spread) in spreads.items():
        noise = np.random.default_rng([zlib.crc32(name.encode()), seed]).standard_normal(out[name].shape)
        drawn = base * np.exp(spread * noise) if base else spread * noise
        out[name] = jnp.asarray(drawn.astype(out[name].dtype))
    for name, factor in factors.items():
        out[name] = (out[name] * factor).astype(out[name].dtype)
    return out
```

```python
from contextlib import ExitStack

import concourse.bass as bass
import numpy as np
from concourse import mybir

F32 = mybir.dt.float32
F32R = mybir.dt.float32r
ALU = mybir.AluOpType
ACT = mybir.ActivationFunctionType

BATCH, FIELDS, EMB, OUT = 2048, 32, 64, 256
PAIRS = FIELDS * (FIELDS - 1) // 2
COLS = 512
TILES = BATCH // COLS
QUADS = FIELDS // 4

MOVING_RING = 8
TERM_RING = 3
PRODUCT_RING = 16
GROUP = 8
WEIGHT_RING = 4
SUM_GROUP = 4
SUM_LAG = 1
PER_BANK = 32


def plan_units():
    units = []
    for j in range(1, FIELDS):
        if j % 4 == 3:
            units += [("diag0", j // 4, j), ("diag1", j // 4, j)]
        units += [("quad", u, j) for u in range(j // 4)]
    return units


UNITS = plan_units()
N = len(UNITS)
GROUPS = N // GROUP
BANKS = N // PER_BANK
SUM_GROUPS = N // SUM_GROUP


def fields_of(unit):
    kind, u, j = unit
    return (4 * u + 1, 4 * u + 2) if kind == "diag1" else (j, j)


FIRST_USE = {j: min(n for n in range(N) if j in fields_of(UNITS[n])) for j in range(1, FIELDS)}
LAST_USE = {j: max(n for n in range(N) if j in fields_of(UNITS[n])) for j in range(1, FIELDS)}


def pair_index(i, j):
    return i * (FIELDS - 1) - i * (i - 1) // 2 + j - i - 1


def chunk_columns(unit, c):
    kind, u, j = unit
    if kind == "quad":
        return [(pair_index(4 * u + t, j), 32 * c + e) for t in range(4) for e in range(32)]
    i, j, n = {("diag0", 0): (4 * u, j, 2), ("diag0", 1): (4 * u + 2, j, 1),
               ("diag1", 0): (4 * u, 4 * u + 1, 1), ("diag1", 1): (4 * u, 4 * u + 2, 2)}[kind, c]
    return [(pair_index(i + t, j), e) if t < n else None for t in range(2) for e in range(EMB)]


def chunk_sums(n, c):
    kind = UNITS[n][0]
    if kind == "quad":
        return n, 0, c == 0
    if kind == "diag0":
        return n, 1 + c, c == 0
    return (n - 1, 3, False) if c == 0 else (n, 1, True)


SEL_WIDTH = 60


def selectors():
    sel = np.zeros((128, 4, SEL_WIDTH), np.float32)
    for t in range(4):
        sel[32 * t:32 * t + 32, 0, 28 + t] = 1
    for t in range(2):
        sel[64 * t:64 * t + 64, 1, 28 + t] = 1
    sel[0:64, 2, 30] = 1
    sel[0:64, 3, 31] = 1
    return sel


def row_of(n):
    return n // PER_BANK, n % 4, 4 * (n % PER_BANK // 4)


def pair_slots():
    slots = np.full((BANKS, 128), -1)
    for n, (kind, u, j) in enumerate(UNITS):
        k, q, r = row_of(n)
        if kind == "quad":
            found = [(t, 4 * u + t, j) for t in range(4)]
        elif kind == "diag0":
            found = [(0, 4 * u, j), (1, 4 * u + 1, j), (2, 4 * u + 2, j), (3, 4 * u, 4 * u + 1)]
        else:
            found = [(t, 4 * u + t, 4 * u + 2) for t in range(2)]
        for t, i, jj in found:
            slots[k, 32 * q + r + t] = pair_index(i, jj)
    return slots


CUT = N - 18


def due_low(j):
    if j > 1:
        return max(due_low(j - 1), slot_due(j))
    return slot_due(1)


def slot_due(j):
    before = j - MOVING_RING
    free = LAST_USE[before] + 1 if before > 0 else LAST_USE[before + FIELDS if before else 24] + 1 - N
    return max(free, FIRST_USE[j] - 16)


def in_window(due, n):
    return (due, 0) if due < CUT else (due - N, 1)


FOLDED_FIRST = [n for n in range(N) if UNITS[n][0] == "quad" and n % 3 == 0]
FOLDED = [n for n in range(N) if UNITS[n][0] == "quad" and n % 4 != 3]


def bass_pair_interactions(nc, x, k, wt, bias, sel, out):
    with ExitStack() as ctx:
        def sb(name, shape, dt=F32):
            return ctx.enter_context(nc.sbuf_tensor(name, shape, dt))

        def sem(name):
            return ctx.enter_context(nc.semaphore(name))

        weights = sb("weights", [128, WEIGHT_RING, GROUP * 256], F32R)
        raw_k = sb("raw_k", [128, 2, GROUP * 256])
        raw_x = sb("raw_x", [128, 2, 2, COLS])
        moving = sb("moving", [128, MOVING_RING, 2, COLS], F32R)
        quad_x = sb("quad_x", [128, QUADS - 1, 2, COLS])
        pair_x = sb("pair_x", [128, 2, 2, COLS])
        products = sb("products", [128, PRODUCT_RING, 2, COLS])
        pair_sums = sb("pair_sums", [128, BANKS, COLS])
        wt_sb = sb("wt_sb", [128, BANKS, OUT])
        bias_sb = sb("bias_sb", [128, 2])
        sel_sb = sb("sel_sb", [128, 4, SEL_WIDTH])
        y_sb = sb("y_sb", [128, 2, COLS])
        split_k = nc.dram_tensor("split_k", [GROUPS, 128, GROUP * 256], F32).ap()

        terms = [ctx.enter_context(nc.psum_tensor(f"terms{i}", [128, 2, COLS], F32)) for i in range(TERM_RING)]
        sums = ctx.enter_context(nc.psum_tensor("sums", [128, COLS], F32))
        y_ps = ctx.enter_context(nc.psum_tensor("y_ps", [128, COLS], F32))

        consts_landed = sem("consts_landed")
        raw_k_landed = [sem(f"raw_k_landed{i}") for i in range(2)]
        raw_x_landed = [sem(f"raw_x_landed{i}") for i in range(2)]
        weights_landed = [sem(f"weights_landed{i}") for i in range(WEIGHT_RING)]
        split_stored = [sem(f"split_stored{i}") for i in range(WEIGHT_RING)]
        quad_x_landed = [sem(f"quad_x_landed{i}") for i in range(QUADS - 1)]
        pair_x_landed = [sem(f"pair_x_landed{i}") for i in range(2)]
        weights_rounded = sem("weights_rounded")
        weights_split = sem("weights_split")
        highs_ready = sem("highs_ready")
        lows_ready = sem("lows_ready")
        terms_ready = sem("terms_ready")
        products_ready = sem("products_ready")
        folds_ready = sem("folds_ready")
        groups_summed = sem("groups_summed")
        sums_ready = sem("sums_ready")
        sums_saved = sem("sums_saved")
        y_ready = sem("y_ready")
        y_saved = sem("y_saved")
        y_stored = [sem(f"y_stored{h}") for h in range(2)]

        def wait(eng, s, tile, per_tile, more):
            if isinstance(tile, int):
                if per_tile * tile + more > 0:
                    eng.wait_ge(s, per_tile * tile + more)
            else:
                eng.wait_ge(s, tile * per_tile + more)

        def each_tile(eng, one_tile):
            one_tile(0, True)
            with eng.Fori(1, TILES) as tile:
                one_tile(tile, False)

        block = ctx.enter_context(nc.Block())

        @block.sync
        def _(sp):
            FJ = FIELDS - 1

            def one_tile(tile, first):
                todo = []
                for g in range(GROUPS):
                    todo.append((GROUP * (g - 4) if first else GROUP * (g - WEIGHT_RING + 1), 2, "k", g))
                    if first:
                        todo.append((GROUP * g, 3, "store", g))
                for p in range(FIELDS // 2):
                    todo.append((max(due_low(max(1, 2 * p)) - 6, due_low(2 * p - 3) if p > 1 else -N), 4, "x", p))
                for u in range(QUADS - 1):
                    todo.append((u - 6 if not first else FIRST_USE[4 * u + 4] - 12, 1, "quad", u))
                for u in range(QUADS):
                    todo.append((FIRST_USE[4 * u + 3] - 14, 1, "pair", u))
                for _, _, kind, a in sorted(todo):
                    if kind == "k" and first:
                        wait(sp, weights_split, 0, 0, a - 1)
                        for h in range(2):
                            sp.dma_start(raw_k[64 * h:64 * h + 64, a % 2, :], k[a]).then_inc(raw_k_landed[a % 2], 16)
                    elif kind == "store":
                        sp.wait_ge(weights_split, a + 1)
                        sp.dma_start(split_k[a], weights[:, a % WEIGHT_RING, :].bitcast(F32)).then_inc(split_stored[a % WEIGHT_RING], 16)
                    elif kind == "k":
                        sp.wait_ge(split_stored[a % WEIGHT_RING], 16 * (GROUPS // WEIGHT_RING))
                        wait(sp, terms_ready, tile, N, GROUP * (a - WEIGHT_RING + 1))
                        sp.dma_start(weights[:, a % WEIGHT_RING, :].bitcast(F32), split_k[a]).then_inc(weights_landed[a % WEIGHT_RING], 16)
                    elif kind == "x":
                        wait(sp, lows_ready, tile, FJ, 2 * a - (3 if a >= 2 else 2))
                        for h in range(2):
                            sp.dma_start(raw_x[64 * h:64 * h + 64, a % 2], x[tile, 2 * a:2 * a + 2].rearrange("f e b -> e f b")
                                         ).then_inc(raw_x_landed[a % 2], 16)
                    elif kind == "quad":
                        wait(sp, products_ready, tile, N, a - (QUADS - 1) + 1)
                        for t in range(4):
                            sp.dma_start(quad_x[32 * t:32 * t + 32, a], x[tile, 4 * a + t].rearrange("(h e) b -> e h b", h=2)
                                         ).then_inc(quad_x_landed[a], 16)
                    else:
                        before = FIRST_USE[4 * a - 5] + 2 if a >= 2 else FIRST_USE[4 * a + 27] + 2 - N
                        wait(sp, products_ready, tile, N, before)
                        for s in range(2):
                            sp.dma_start(pair_x[64 * s:64 * s + 64, a % 2], x[tile, 4 * a + s:4 * a + s + 3:2].rearrange("m e b -> e m b")
                                         ).then_inc(pair_x_landed[a % 2], 16)

            each_tile(sp, one_tile)

        @block.tensor
        def _(pe):
            def sum_group(tile, g):
                group = range(SUM_GROUP * g, SUM_GROUP * (g + 1))
                if SUM_GROUP * g % PER_BANK == 0:
                    wait(pe, sums_saved, tile, BANKS, SUM_GROUP * g // PER_BANK)
                for n in [n for n in group if n in FOLDED][-1:]:
                    wait(pe, folds_ready, tile, len(FOLDED), FOLDED.index(n) + 1)
                for n in [n for n in group if n not in FOLDED][-1:]:
                    wait(pe, products_ready, tile, N, n + 1)
                for c in range(2):
                    for n in group:
                        if c == 1 and n in FOLDED:
                            continue
                        at, s, first = chunk_sums(n, c)
                        _, q, r = row_of(at)
                        last = pe.matmul(sums[32 * q:32 * q + 32, :], sel_sb[:, s, 28 - r:60 - r],
                                         products[:, n % PRODUCT_RING, c, :], start=first and at % PER_BANK < 4,
                                         stop=False, tile_position=(0, 32 * q), skip_group_check=True)
                last.then_inc(groups_summed, 1)

            def y_part(tile, h, k):
                if h == 0 and k == 0:
                    wait(pe, sums_saved, tile, BANKS, BANKS)
                if k == 0:
                    wait(pe, y_saved, tile, 2, h)
                mm = pe.matmul(y_ps[:, :], wt_sb[:, k, 128 * h:128 * h + 128], pair_sums[:, k, :],
                               start=k == 0, stop=k == BANKS - 1)
                if k == BANKS - 1:
                    mm.then_inc(y_ready, 1)

            def one_tile(tile, first):
                for n, unit in enumerate(UNITS):
                    if n % GROUP == 0:
                        g = n // GROUP
                        if first:
                            pe.wait_ge(weights_split, g + 1)
                        else:
                            per = GROUPS // WEIGHT_RING
                            wait(pe, weights_landed[g % WEIGHT_RING], tile, 16 * per, 16 * (g // WEIGHT_RING + 1 - per))
                    new = [j for j in FIRST_USE if FIRST_USE[j] == n]
                    if new:
                        wait(pe, lows_ready, tile, FIELDS - 1, max(new))
                    wait(pe, products_ready, tile, N, n - 2 if n >= 3 else {0: -1, 1: 0, 2: -2}[n])
                    for c in range(2):
                        w = weights[:, n // GROUP % WEIGHT_RING, 256 * (n % GROUP) + 128 * c:256 * (n % GROUP) + 128 * c + 128]
                        for part in range(2):
                            mm = pe.matmul(terms[n % TERM_RING][:, c, :], w, moving[:, fields_of(unit)[c] % MOVING_RING, part, :],
                                           start=part == 0, stop=part == 1)
                    mm.then_inc(terms_ready, 1)
                    if n % SUM_GROUP == SUM_GROUP - 1:
                        g = n // SUM_GROUP - SUM_LAG
                        if g >= 0:
                            sum_group(tile, g)
                        elif not first:
                            sum_group(tile - 1, g + SUM_GROUPS)
                    if not first and n in Y_AT:
                        y_part(tile - 1, *Y_AT[n])

            pe.wait_ge(consts_landed, 48)
            each_tile(pe, one_tile)
            for g in range(SUM_GROUPS - SUM_LAG, SUM_GROUPS):
                sum_group(TILES - 1, g)
            for h in range(2):
                for k in range(BANKS):
                    y_part(TILES - 1, h, k)

        @block.vector
        def _(dve):
            def one_tile(tile, first):
                for n, (kind, u, j) in enumerate(UNITS):
                    if kind == "quad" and j == 4 * u + 4:
                        wait(dve, quad_x_landed[u], tile, 64, 64)
                    if kind == "diag0":
                        per = QUADS // 2
                        wait(dve, pair_x_landed[u % 2], tile, 32 * per, 32 * (u // 2 + 1))
                    wait(dve, groups_summed, tile, SUM_GROUPS, (n - PRODUCT_RING) // SUM_GROUP + 1)
                    wait(dve, terms_ready, tile, N, n + 1)
                    if kind == "quad":
                        xi = quad_x[:, u]
                    elif kind == "diag0":
                        xi = pair_x[:, u % 2]
                    else:
                        xi = pair_x[:, u % 2, 0:1, :].broadcast_to([128, 2, COLS])
                    nc.vector.tensor_tensor(products[:, n % PRODUCT_RING], terms[n % TERM_RING][:, :, :], xi,
                                            ALU.mult).then_inc(products_ready, 1)

            each_tile(dve, one_tile)

        @block.gpsimd
        def _(pool):
            def low(tile, j):
                wait(pool, highs_ready, tile, FIELDS - 1, j)
                nc.gpsimd.tensor_tensor(moving[:, j % MOVING_RING, 1, :], raw_x[:, j // 2 % 2, j % 2, :],
                                        moving[:, j % MOVING_RING, 0, :].bitcast(F32), ALU.subtract).then_inc(lows_ready, 1)

            def low_k(g, lows, folds):
                wait(pool, lows_ready, 0, 0, lows)
                wait(pool, folds_ready, 0, 0, folds)
                pool.wait_ge(weights_rounded, g + 1)
                w = weights[64:128, g % WEIGHT_RING, :]
                nc.gpsimd.tensor_tensor(w, raw_k[64:128, g % 2, :], w.bitcast(F32), ALU.subtract).then_inc(weights_split, 1)
                pool.wait_ge(weights_split, g + 1)

            def fold(tile, n):
                wait(pool, products_ready, tile, N, n + 1)
                z = products[:, n % PRODUCT_RING]
                nc.gpsimd.tensor_tensor(z[:, 0, :], z[:, 0, :], z[:, 1, :], ALU.add).then_inc(folds_ready, 1)

            def one_tile(tile, first):
                todo = [(*in_window(due_low(j), 0), "low", j) for j in range(1, FIELDS)]
                todo += [(*in_window(n + 2, 0), "fold", n) for n in FOLDED]
                if first:
                    todo += [(GROUP * (g - 2) - 1, 0, "low_k", g) for g in range(GROUPS)]
                lows = folds = 0
                for _, back, kind, a in sorted(todo):
                    if kind == "low_k":
                        low_k(a, lows, folds)
                    elif kind == "low":
                        low(tile, a)
                        lows += 1
                    elif not (first and back):
                        fold(tile - back, a)
                        folds += 1

            each_tile(pool, one_tile)
            for n in FOLDED:
                if n + 2 >= CUT:
                    fold(TILES - 1, n)

        @block.scalar
        def _(act):
            act.dma_start(sel_sb[:], sel).then_inc(consts_landed, 16)
            act.dma_start(wt_sb[:], wt).then_inc(consts_landed, 16)
            act.dma_start(bias_sb[:], bias).then_inc(consts_landed, 16)

            def high(tile, j):
                per = FIELDS // 4
                wait(act, raw_x_landed[j // 2 % 2], tile, 32 * per, 32 * (j // 4 + 1))
                before = j - MOVING_RING
                wait(act, terms_ready, tile, N, LAST_USE[before] + 1 if before > 0 else
                     LAST_USE[before + FIELDS if before else 24] + 1 - N)
                nc.scalar.copy(moving[:, j % MOVING_RING, 0, :], raw_x[:, j // 2 % 2, j % 2, :]).then_inc(highs_ready, 1)

            def round_k(g):
                act.wait_ge(raw_k_landed[g % 2], 32 * (g // 2 + 1))
                if g >= WEIGHT_RING:
                    act.wait_ge(terms_ready, GROUP * (g - WEIGHT_RING + 1))
                    act.wait_ge(split_stored[g % WEIGHT_RING], 16 * (g // WEIGHT_RING))
                nc.scalar.copy(weights[:, g % WEIGHT_RING, :], raw_k[:, g % 2, :]).then_inc(weights_rounded, 1)

            def save_sums(tile, k):
                wait(act, groups_summed, tile, SUM_GROUPS, (k + 1) * PER_BANK // SUM_GROUP)
                wait(act, y_ready, tile, 2, 0)
                nc.scalar.copy(pair_sums[:, k, :], sums[:, :]).then_inc(sums_saved, 1)

            def save_y(tile, h):
                wait(act, y_ready, tile, 2, h + 1)
                wait(act, y_stored[h], tile, 16, 0)
                nc.scalar.activation(y_sb[:, h, :], y_ps[:, :], ACT.Identity, bias=bias_sb[:, h:h + 1]).then_inc(y_saved, 1)
                wait(act, y_saved, tile, 2, h + 1)
                act.dma_start(out[h, tile], y_sb[:, h, :]).then_inc(y_stored[h], 16)

            def one_tile(tile, first):
                todo = [(*in_window(due_low(j) - 1, 0), "high", j) for j in range(1, FIELDS)]
                todo += [(*in_window(PER_BANK * (k + 1) + SUM_GROUP * SUM_LAG, 0), "sums", k) for k in range(BANKS)]
                todo += [(max(n for n in Y_AT if Y_AT[n][0] == h) + 1, 1, "y", h) for h in range(2)]
                if first:
                    todo += [(GROUP * (g - 2) - 2, 0, "round_k", g) for g in range(GROUPS)]
                for _, back, kind, a in sorted(todo):
                    if kind == "high":
                        high(tile, a)
                    elif kind == "round_k":
                        round_k(a)
                    elif not (first and back):
                        (save_sums if kind == "sums" else save_y)(tile - back, a)

            each_tile(act, one_tile)
            save_sums(TILES - 1, BANKS - 1)
            for h in range(2):
                save_y(TILES - 1, h)
            for h in range(2):
                act.wait_ge(y_stored[h], 16 * TILES)


Y_AT = {14: (0, 0), 16: (0, 1), 18: (0, 2), 20: (0, 3), 25: (1, 0), 27: (1, 1), 29: (1, 2), 31: (1, 3)}


def kernel(r_feat_emb, L0_rec_kernel, L0_rec_W, L0_rec_b):
    import concourse.bacc as bacc
    from concourse.bass_utils import run_bass_kernel_spmd

    x = np.ascontiguousarray(np.asarray(r_feat_emb).reshape(TILES, COLS, FIELDS, EMB).transpose(0, 2, 3, 1))
    cols = [col for unit in UNITS for c in range(2) for col in chunk_columns(unit, c)]
    at = [n for n, col in enumerate(cols) if col is not None]
    flat = np.asarray(L0_rec_kernel).reshape(EMB, PAIRS * EMB)
    k = np.zeros((EMB, len(cols)), flat.dtype)
    k[:, at] = flat[:, [cols[n][0] * EMB + cols[n][1] for n in at]]
    k = np.ascontiguousarray(k.reshape(EMB, GROUPS, -1).transpose(1, 0, 2))
    slots = pair_slots().T
    w = np.asarray(L0_rec_W)
    wt = np.zeros((128, BANKS, OUT), w.dtype)
    wt[slots >= 0] = w.T[slots[slots >= 0]]
    bias = np.ascontiguousarray(np.asarray(L0_rec_b).reshape(2, 128).T)
    arrays = {"x": x, "k": k, "wt": wt, "bias": bias, "sel": selectors()}

    nc = bacc.Bacc("TRN2", target_bir_lowering=False, num_devices=1)
    args = [nc.dram_tensor(f"in_{n}", a.shape, mybir.dt.from_np(a.dtype), kind="ExternalInput").ap()
            for n, a in arrays.items()]
    out = nc.dram_tensor("out_y", [2, TILES, 128, COLS], F32, kind="ExternalOutput").ap()
    bass_pair_interactions(nc, *args, out)
    r = run_bass_kernel_spmd(nc, [{f"in_{n}": a for n, a in arrays.items()}], core_ids=[0])
    y = np.asarray(r.results[0]["out_y"])
    return np.ascontiguousarray(y.transpose(1, 3, 0, 2).reshape(BATCH, OUT))
```

```python
from contextlib import ExitStack

import concourse.bass as bass
import numpy as np
from concourse import mybir

F32 = mybir.dt.float32
F32R = mybir.dt.float32r
ALU = mybir.AluOpType
ACT = mybir.ActivationFunctionType

BATCH, FIELDS, EMB, OUT = 2048, 32, 64, 256
PAIRS = FIELDS * (FIELDS - 1) // 2
COLS = 512
TILES = BATCH // COLS
QUADS = FIELDS // 4

MOVING_SLOTS = 12
TERM_RING = 3
PRODUCT_RING = 16
PAIR_RING = 2
GROUP = 4
WEIGHT_RING = 4
RAW_RING = 4
SUM_GROUP = 4
SUM_LAG = 3
UNFOLDED = (8, 20)
PER_BANK = 32


QUAD_ORDER = (4, 3, 5, 2, 6, 1, 7, 0)
SLOT_OF_QUAD = {4: 0, 2: 0, 1: 0, 3: 1, 6: 1, 0: 1, 5: 2, 7: 2}


def plan_units():
    units = []

    def diagonals(*quads):
        for v in quads:
            units.extend([("diag0", v, 4 * v + 3), ("diag1", v, 4 * v + 3)])

    for v in QUAD_ORDER[:-1]:
        for u in range(v):
            units += [("quad", u, 4 * v + t) for t in range(4)]
            if (v, u) == (7, 3):
                diagonals(7, 0)
        before = QUAD_ORDER[QUAD_ORDER.index(v) - 1]
        if v in QUAD_ORDER[1:-1:2]:
            diagonals(before, v)
    return units


UNITS = plan_units()
N = len(UNITS)
GROUPS = N // GROUP
BANKS = N // PER_BANK
SUM_GROUPS = N // SUM_GROUP


def fields_of(unit):
    kind, u, j = unit
    return (4 * u + 1, 4 * u + 2) if kind == "diag1" else (j, j)


FIRST_USE = {j: min(n for n in range(N) if j in fields_of(UNITS[n])) for j in range(1, FIELDS)}
LAST_USE = {j: max(n for n in range(N) if j in fields_of(UNITS[n])) for j in range(1, FIELDS)}


def pair_index(i, j):
    return i * (FIELDS - 1) - i * (i - 1) // 2 + j - i - 1


def chunk_columns(unit, c):
    kind, u, j = unit
    if kind == "quad":
        return [(pair_index(4 * u + t, j), 32 * c + e) for t in range(4) for e in range(32)]
    i, j, n = {("diag0", 0): (4 * u, j, 2), ("diag0", 1): (4 * u + 2, j, 1),
               ("diag1", 0): (4 * u, 4 * u + 1, 1), ("diag1", 1): (4 * u, 4 * u + 2, 2)}[kind, c]
    return [(pair_index(i + t, j), e) if t < n else None for t in range(2) for e in range(EMB)]


def chunk_sums(n, c):
    kind = UNITS[n][0]
    if kind == "quad":
        return n, 0, c == 0
    if kind == "diag0":
        return n, 1 + c, c == 0
    return (n - 1, 3, False) if c == 0 else (n, 1, True)


SEL_WIDTH = 60


def selectors():
    sel = np.zeros((128, 4, SEL_WIDTH), np.float32)
    for t in range(4):
        sel[32 * t:32 * t + 32, 0, 28 + t] = 1
    for t in range(2):
        sel[64 * t:64 * t + 64, 1, 28 + t] = 1
    sel[0:64, 2, 30] = 1
    sel[0:64, 3, 31] = 1
    return sel


def row_of(n):
    return n // PER_BANK, n % 4, 4 * (n % PER_BANK // 4)


def pair_slots():
    slots = np.full((BANKS, 128), -1)
    for n, (kind, u, j) in enumerate(UNITS):
        k, q, r = row_of(n)
        if kind == "quad":
            found = [(t, 4 * u + t, j) for t in range(4)]
        elif kind == "diag0":
            found = [(0, 4 * u, j), (1, 4 * u + 1, j), (2, 4 * u + 2, j), (3, 4 * u, 4 * u + 1)]
        else:
            found = [(t, 4 * u + t, 4 * u + 2) for t in range(2)]
        for t, i, jj in found:
            slots[k, 32 * q + r + t] = pair_index(i, jj)
    return slots


LOADS = sorted(range(FIELDS // 2), key=lambda p: min(FIRST_USE[j] for j in (2 * p, 2 * p + 1) if j))
MADE = [j for p in LOADS for j in (2 * p, 2 * p + 1) if j]
RANK = {j: n for n, j in enumerate(MADE)}


def fields_in(p):
    return [j for j in (2 * p, 2 * p + 1) if j]


DIAGONAL = [UNITS.index(("diag0", u, 4 * u + 3)) for u in QUAD_ORDER]
QUAD_USES = [[n for n in range(N) if UNITS[n][:2] == ("quad", u)] for u in range(QUADS - 1)]


def moving_slot(j):
    return 4 * SLOT_OF_QUAD[j // 4] + j % 4


def slot_free(j):
    before = sorted((i for i in MADE if moving_slot(i) == moving_slot(j)), key=FIRST_USE.get)
    at = before.index(j)
    return LAST_USE[before[at - 1]] + 1 - (0 if at else N)


CUT = N - 18
LEAD = 12
DUE = {j: max(max(slot_free(i), FIRST_USE[i] - LEAD) for i in MADE[:RANK[j] + 1]) for j in MADE}


def in_window(due):
    return (due, 0) if due < CUT else (due - N, 1)


QUAD_GROUPS = [g for g in range(SUM_GROUPS) if UNITS[SUM_GROUP * g][0] == "quad"]
FOLDED = [g for g in QUAD_GROUPS if g not in UNFOLDED]
FOLDED_FIRST = [g for g in FOLDED if g >= 26 or g % 2]


def split_by_vector(g):
    return g < 3 or g % 4 == 0


def bass_pair_interactions(nc, x, x_quads, x_pairs, k, wt, bias, sel, out):
    with ExitStack() as ctx:
        def sb(name, shape, dt=F32):
            return ctx.enter_context(nc.sbuf_tensor(name, shape, dt))

        def sem(name):
            return ctx.enter_context(nc.semaphore(name))

        weights = sb("weights", [128, WEIGHT_RING, GROUP * 256], F32R)
        raw_k = sb("raw_k", [128, RAW_RING, GROUP * 256])
        raw_x = sb("raw_x", [128, 2, 2, COLS])
        moving = sb("moving", [128, MOVING_SLOTS, 2, COLS], F32R)
        quad_x = sb("quad_x", [128, QUADS - 1, 2, COLS])
        pair_x = sb("pair_x", [128, PAIR_RING, 2, COLS])
        products = sb("products", [128, PRODUCT_RING, 2, COLS])
        pair_sums = sb("pair_sums", [128, BANKS, COLS])
        wt_sb = sb("wt_sb", [128, BANKS, OUT])
        bias_sb = sb("bias_sb", [128, 2])
        sel_sb = sb("sel_sb", [128, 4, SEL_WIDTH])
        y_sb = sb("y_sb", [128, 2, COLS])
        split_k = nc.dram_tensor("split_k", [GROUPS, 128, GROUP * 256], F32).ap()

        terms = [ctx.enter_context(nc.psum_tensor(f"terms{i}", [128, 2, COLS], F32)) for i in range(TERM_RING)]
        sums = ctx.enter_context(nc.psum_tensor("sums", [128, COLS], F32))
        y_ps = ctx.enter_context(nc.psum_tensor("y_ps", [128, COLS], F32))

        consts_landed = sem("consts_landed")
        raw_k_landed = [sem(f"raw_k_landed{i}") for i in range(RAW_RING)]
        raw_x_landed = [sem(f"raw_x_landed{i}") for i in range(2)]
        weights_landed = [sem(f"weights_landed{i}") for i in range(WEIGHT_RING)]
        split_stored = [sem(f"split_stored{i}") for i in range(WEIGHT_RING)]
        quad_x_landed = [sem(f"quad_x_landed{i}") for i in range(QUADS - 1)]
        pair_x_landed = [sem(f"pair_x_landed{i}") for i in range(PAIR_RING)]
        weights_rounded = sem("weights_rounded")
        weights_split = sem("weights_split")
        weights_split_dve = sem("weights_split_dve")
        highs_ready = sem("highs_ready")
        lows_ready = sem("lows_ready")
        terms_ready = sem("terms_ready")
        products_ready = sem("products_ready")
        folds_ready = sem("folds_ready")
        groups_summed = sem("groups_summed")
        sums_ready = sem("sums_ready")
        sums_saved = sem("sums_saved")
        y_ready = sem("y_ready")
        y_saved = sem("y_saved")
        y_stored = [sem(f"y_stored{h}") for h in range(2)]

        def wait(eng, s, tile, per_tile, more):
            if isinstance(tile, int):
                if per_tile * tile + more > 0:
                    eng.wait_ge(s, per_tile * tile + more)
            else:
                eng.wait_ge(s, tile * per_tile + more)

        def wait_split(eng, g):
            mine = sum(split_by_vector(f) == split_by_vector(g) for f in range(g + 1))
            eng.wait_ge(weights_split_dve if split_by_vector(g) else weights_split, mine)

        def wait_folded(eng, tile, g):
            if isinstance(tile, int) and tile == 0:
                eng.wait_ge(folds_ready, FOLDED_FIRST.index(g) + 1)
            else:
                wait(eng, folds_ready, tile, len(FOLDED), len(FOLDED_FIRST) - len(FOLDED) + FOLDED.index(g) + 1)

        def each_tile(eng, one_tile):
            one_tile(0, True)
            with eng.Fori(1, TILES) as tile:
                one_tile(tile, False)

        block = ctx.enter_context(nc.Block())

        @block.sync
        def _(sp):
            def one_tile(tile, first):
                todo = []
                for g in range(GROUPS):
                    raw_due = {0: -N, 1: -9, 2: -8, 3: -7}.get(g, GROUP * (g - 5) + 2)
                    todo.append((raw_due if first else GROUP * (g - WEIGHT_RING + 1), 2, "k", g))
                for n, p in enumerate(LOADS):
                    if first and n < 2:
                        due = (-N + 1, -10)[n]
                    else:
                        due = max(DUE[max(1, 2 * p)] - 4, DUE[fields_in(LOADS[n - 2])[-1]] - (0 if n > 1 else N))
                    todo.append((due, 4, "x", n))
                for u in range(QUADS - 1):
                    todo.append((QUAD_USES[u][0] - 16 + 2 * u if first else QUAD_USES[u][-1] + 1 - N, 1, "quad", u))
                for u in range(QUADS):
                    todo.append((DIAGONAL[u] - 16, 1, "pair", u))
                for _, _, kind, a in sorted(todo):
                    if kind == "k" and first:
                        if a >= RAW_RING:
                            wait_split(sp, a - RAW_RING)
                        for h in range(2):
                            sp.dma_start(raw_k[64 * h:64 * h + 64, a % RAW_RING, :], k[a]).then_inc(raw_k_landed[a % RAW_RING], 16)
                    elif kind == "k":
                        sp.wait_ge(split_stored[a % WEIGHT_RING], 16 * (GROUPS // WEIGHT_RING))
                        wait(sp, terms_ready, tile, N, GROUP * (a - WEIGHT_RING + 1))
                        sp.dma_start(weights[:, a % WEIGHT_RING, :].bitcast(F32), split_k[a]).then_inc(weights_landed[a % WEIGHT_RING], 16)
                    elif kind == "x":
                        at = (tile * FIELDS + 2 * LOADS[a]) * EMB * COLS
                        source = x[at:at + 2 * EMB * COLS] if first else x[bass.ds(sp.snap(at), 2 * EMB * COLS)]
                        last = fields_in(LOADS[a - 2])[-1]
                        wait(sp, lows_ready, tile, len(MADE), RANK[last] + 1 - (0 if a > 1 else len(MADE)))
                        for h in range(2):
                            sp.dma_start(raw_x[64 * h:64 * h + 64, a % 2], source.rearrange("(f e b) -> e f b", f=2, b=COLS)
                                         ).then_inc(raw_x_landed[a % 2], 16)
                    elif kind == "quad":
                        wait(sp, products_ready, tile, N, QUAD_USES[a][-1] + 1 - N)
                        sp.dma_start(quad_x[:, a], x_quads[tile, a]).then_inc(quad_x_landed[a], 16)
                    else:
                        at = (tile * QUADS + QUAD_ORDER[a]) * 256 * COLS
                        source = x_pairs[at:at + 256 * COLS] if first else x_pairs[bass.ds(sp.snap(at), 256 * COLS)]
                        wait(sp, products_ready, tile, N, DIAGONAL[a - PAIR_RING] + 2 - (0 if a >= PAIR_RING else N))
                        sp.dma_start(pair_x[:, a % PAIR_RING], source.rearrange("(p m b) -> p m b", m=2, b=COLS)
                                     ).then_inc(pair_x_landed[a % PAIR_RING], 16)

            each_tile(sp, one_tile)

        @block.tensor
        def _(pe):
            def sum_group(tile, g):
                if isinstance(tile, int) and tile == 0 and g == 0:
                    pe.wait_ge(consts_landed, 48)
                group = range(SUM_GROUP * g, SUM_GROUP * (g + 1))
                if SUM_GROUP * g % PER_BANK == 0:
                    wait(pe, sums_saved, tile, BANKS, SUM_GROUP * g // PER_BANK)
                if g in (FOLDED_FIRST if isinstance(tile, int) and tile == 0 else FOLDED):
                    wait_folded(pe, tile, g)
                    chunks = [0]
                else:
                    wait(pe, products_ready, tile, N, SUM_GROUP * (g + 1))
                    chunks = [0, 1]
                for c in chunks:
                    for n in group:
                        at, s, first = chunk_sums(n, c)
                        _, q, r = row_of(at)
                        last = pe.matmul(sums[32 * q:32 * q + 32, :], sel_sb[:, s, 28 - r:60 - r],
                                         products[:, n % PRODUCT_RING, c, :], start=first and at % PER_BANK < 4,
                                         stop=False, tile_position=(0, 32 * q), skip_group_check=True)
                last.then_inc(groups_summed, 1)

            def y_part(tile, h, k):
                if h == 0 and k == 0:
                    wait(pe, sums_saved, tile, BANKS, BANKS)
                if k == 0:
                    wait(pe, y_saved, tile, 2, h)
                mm = pe.matmul(y_ps[:, :], wt_sb[:, k, 128 * h:128 * h + 128], pair_sums[:, k, :],
                               start=k == 0, stop=k == BANKS - 1)
                if k == BANKS - 1:
                    mm.then_inc(y_ready, 1)

            def one_tile(tile, first):
                for n, unit in enumerate(UNITS):
                    if n % GROUP == 0:
                        g = n // GROUP
                        if first:
                            wait_split(pe, g)
                        else:
                            per = GROUPS // WEIGHT_RING
                            wait(pe, weights_landed[g % WEIGHT_RING], tile, 16 * per, 16 * (g // WEIGHT_RING + 1 - per))
                    new = [j for j in FIRST_USE if FIRST_USE[j] == n]
                    if new:
                        wait(pe, lows_ready, tile, len(MADE), max(RANK[j] for j in new) + 1)
                    wait(pe, products_ready, tile, N, n - 2 if n >= 3 else {0: -1, 1: 0, 2: -2}[n])
                    for c in range(2):
                        w = weights[:, n // GROUP % WEIGHT_RING, 256 * (n % GROUP) + 128 * c:256 * (n % GROUP) + 128 * c + 128]
                        for part in range(2):
                            mm = pe.matmul(terms[n % TERM_RING][:, c, :], w, moving[:, moving_slot(fields_of(unit)[c]), part, :],
                                           start=part == 0, stop=part == 1)
                    mm.then_inc(terms_ready, 1)
                    if n % SUM_GROUP == SUM_GROUP - 1:
                        g = n // SUM_GROUP - SUM_LAG
                        if g >= 0:
                            sum_group(tile, g)
                        elif not first:
                            sum_group(tile - 1, g + SUM_GROUPS)
                    if not first and n in Y_AT:
                        y_part(tile - 1, *Y_AT[n])

            each_tile(pe, one_tile)
            for g in range(SUM_GROUPS - SUM_LAG, SUM_GROUPS):
                sum_group(TILES - 1, g)
            for h in range(2):
                for k in range(BANKS):
                    y_part(TILES - 1, h, k)

        @block.vector
        def _(dve):
            def low_k(g):
                dve.wait_ge(weights_rounded, g + 1)
                w = weights[64:128, g % WEIGHT_RING, :]
                nc.vector.tensor_tensor(w, raw_k[64:128, g % RAW_RING, :], w.bitcast(F32), ALU.subtract).then_inc(weights_split_dve, 1)

            def one_tile(tile, first):
                for n, (kind, u, j) in enumerate(UNITS):
                    for g in range(GROUPS):
                        if first and split_by_vector(g) and n == max(0, g, GROUP * (g - 3) + 2):
                            low_k(g)
                    if kind == "quad" and n == QUAD_USES[u][0]:
                        wait(dve, quad_x_landed[u], tile, 16, 16)
                    if kind == "diag0":
                        per = QUADS // PAIR_RING
                        d = QUAD_ORDER.index(u)
                        wait(dve, pair_x_landed[d % PAIR_RING], tile, 16 * per, 16 * (d // PAIR_RING + 1))
                    wait(dve, groups_summed, tile, SUM_GROUPS, (n - PRODUCT_RING) // SUM_GROUP + 1)
                    wait(dve, terms_ready, tile, N, n + 1)
                    if kind == "quad":
                        xi = quad_x[:, u]
                    elif kind == "diag0":
                        xi = pair_x[:, d % PAIR_RING]
                    else:
                        xi = pair_x[:, d % PAIR_RING, 0:1, :].broadcast_to([128, 2, COLS])
                    nc.vector.tensor_tensor(products[:, n % PRODUCT_RING], terms[n % TERM_RING][:, :, :], xi,
                                            ALU.mult).then_inc(products_ready, 1)

            each_tile(dve, one_tile)

        @block.gpsimd
        def _(pool):
            def low(tile, j):
                wait(pool, highs_ready, tile, len(MADE), RANK[j] + 1)
                at = moving_slot(j)
                nc.gpsimd.tensor_tensor(moving[:, at, 1, :], raw_x[:, LOADS.index(j // 2) % 2, j % 2, :],
                                        moving[:, at, 0, :].bitcast(F32), ALU.subtract).then_inc(lows_ready, 1)

            def low_k(g, lows, folds):
                wait(pool, lows_ready, 0, 0, lows)
                wait(pool, folds_ready, 0, 0, folds)
                pool.wait_ge(weights_rounded, g + 1)
                w = weights[64:128, g % WEIGHT_RING, :]
                nc.gpsimd.tensor_tensor(w, raw_k[64:128, g % RAW_RING, :], w.bitcast(F32), ALU.subtract).then_inc(weights_split, 1)
                wait_split(pool, g)

            def fold(tile, g):
                wait(pool, products_ready, tile, N, SUM_GROUP * (g + 1))
                at = SUM_GROUP * g % PRODUCT_RING
                z = products[:, at:at + SUM_GROUP]
                nc.gpsimd.tensor_tensor(z[:, :, 0, :], z[:, :, 0, :], z[:, :, 1, :], ALU.add).then_inc(folds_ready, 1)

            def one_tile(tile, first):
                todo = [(*in_window(DUE[j]), "low", RANK[j]) for j in MADE]
                todo += [(*in_window(SUM_GROUP * (g + 1) + 1), "fold", g) for g in (FOLDED_FIRST if first else FOLDED)]
                if first:
                    todo += [(GROUP * (g - 3) + 1, 0, "low_k", g) for g in range(GROUPS) if not split_by_vector(g)]
                lows = folds = 0
                for _, back, kind, a in sorted(todo):
                    if kind == "low_k":
                        low_k(a, lows, folds)
                    elif kind == "low":
                        low(tile, MADE[a])
                        lows += 1
                    elif not (first and back):
                        fold(tile - back, a)
                        folds += 1

            each_tile(pool, one_tile)
            for g in FOLDED:
                if in_window(SUM_GROUP * (g + 1) + 1)[1]:
                    fold(TILES - 1, g)

        @block.scalar
        def _(act):
            def high(tile, j):
                at = LOADS.index(j // 2)
                per = len(LOADS) // 2
                wait(act, raw_x_landed[at % 2], tile, 32 * per, 32 * (at // 2 + 1))
                wait(act, terms_ready, tile, N, slot_free(j))
                nc.scalar.copy(moving[:, moving_slot(j), 0, :], raw_x[:, at % 2, j % 2, :]).then_inc(highs_ready, 1)

            def round_k(g):
                act.wait_ge(raw_k_landed[g % RAW_RING], 32 * (g // RAW_RING + 1))
                if g >= WEIGHT_RING:
                    act.wait_ge(terms_ready, GROUP * (g - WEIGHT_RING + 1))
                    act.wait_ge(split_stored[g % WEIGHT_RING], 16 * (g // WEIGHT_RING))
                nc.scalar.copy(weights[:, g % WEIGHT_RING, :], raw_k[:, g % RAW_RING, :]).then_inc(weights_rounded, 1)

            def save_sums(tile, k):
                wait(act, groups_summed, tile, SUM_GROUPS, (k + 1) * PER_BANK // SUM_GROUP)
                wait(act, y_ready, tile, 2, 0)
                nc.scalar.copy(pair_sums[:, k, :], sums[:, :]).then_inc(sums_saved, 1)

            def save_y(tile, h):
                wait(act, y_ready, tile, 2, h + 1)
                wait(act, y_stored[h], tile, 16, 0)
                nc.scalar.activation(y_sb[:, h, :], y_ps[:, :], ACT.Identity, bias=bias_sb[:, h:h + 1]).then_inc(y_saved, 1)
                wait(act, y_saved, tile, 2, h + 1)
                act.dma_start(out[h, tile], y_sb[:, h, :]).then_inc(y_stored[h], 16)

            def one_tile(tile, first):
                todo = [(*in_window(DUE[j] - 1), "high", RANK[j]) for j in MADE]
                todo += [(*in_window(PER_BANK * (k + 1) + SUM_GROUP * SUM_LAG - 1), "sums", k) for k in range(BANKS)]
                todo += [(max(n for n in Y_AT if Y_AT[n][0] == h) + 1, 1, "y", h) for h in range(2)]
                if first:
                    todo += [(GROUP * (g - 3), 0, "round_k", g) for g in range(GROUPS)]
                    todo += [(GROUP * (g - 3) + (4 if split_by_vector(g) else 6), 0, "store_k", g) for g in range(GROUPS)]
                    todo += [(0, 0, "consts", a) for a in range(3)]
                for _, back, kind, a in sorted(todo):
                    if kind == "high":
                        high(tile, MADE[a])
                    elif kind == "round_k":
                        round_k(a)
                    elif kind == "store_k":
                        wait_split(act, a)
                        act.dma_start(split_k[a], weights[:, a % WEIGHT_RING, :].bitcast(F32)).then_inc(split_stored[a % WEIGHT_RING], 16)
                    elif kind == "consts":
                        chip, dram = ((sel_sb, sel), (wt_sb, wt), (bias_sb, bias))[a]
                        act.dma_start(chip[:], dram).then_inc(consts_landed, 16)
                    elif not (first and back):
                        (save_sums if kind == "sums" else save_y)(tile - back, a)

            each_tile(act, one_tile)
            save_sums(TILES - 1, BANKS - 1)
            for h in range(2):
                save_y(TILES - 1, h)
            for h in range(2):
                act.wait_ge(y_stored[h], 16 * TILES)


Y_AT = {14: (0, 0), 16: (0, 1), 18: (0, 2), 20: (0, 3), 25: (1, 0), 27: (1, 1), 29: (1, 2), 31: (1, 3)}


def kernel(r_feat_emb, L0_rec_kernel, L0_rec_W, L0_rec_b):
    import concourse.bacc as bacc
    from concourse.bass_utils import run_bass_kernel_spmd

    x = np.ascontiguousarray(np.asarray(r_feat_emb).reshape(TILES, COLS, FIELDS, EMB).transpose(0, 2, 3, 1))
    x_quads = x.reshape(TILES, QUADS, 4, 2, 32, COLS)[:, :QUADS - 1].transpose(0, 1, 2, 4, 3, 5)
    x_quads = np.ascontiguousarray(x_quads.reshape(TILES, QUADS - 1, 128, 2, COLS))
    x_pairs = np.ascontiguousarray(x.reshape(TILES, QUADS, 2, 2, EMB, COLS).transpose(0, 1, 3, 4, 2, 5)).reshape(-1)
    cols = [col for unit in UNITS for c in range(2) for col in chunk_columns(unit, c)]
    at = [n for n, col in enumerate(cols) if col is not None]
    flat = np.asarray(L0_rec_kernel).reshape(EMB, PAIRS * EMB)
    k = np.zeros((EMB, len(cols)), flat.dtype)
    k[:, at] = flat[:, [cols[n][0] * EMB + cols[n][1] for n in at]]
    k = np.ascontiguousarray(k.reshape(EMB, GROUPS, -1).transpose(1, 0, 2))
    slots = pair_slots().T
    w = np.asarray(L0_rec_W)
    wt = np.zeros((128, BANKS, OUT), w.dtype)
    wt[slots >= 0] = w.T[slots[slots >= 0]]
    bias = np.ascontiguousarray(np.asarray(L0_rec_b).reshape(2, 128).T)
    arrays = {"x": x.reshape(-1), "x_quads": x_quads, "x_pairs": x_pairs, "k": k, "wt": wt, "bias": bias, "sel": selectors()}

    nc = bacc.Bacc("TRN2", target_bir_lowering=False, num_devices=1)
    args = [nc.dram_tensor(f"in_{n}", a.shape, mybir.dt.from_np(a.dtype), kind="ExternalInput").ap()
            for n, a in arrays.items()]
    out = nc.dram_tensor("out_y", [2, TILES, 128, COLS], F32, kind="ExternalOutput").ap()
    bass_pair_interactions(nc, *args, out)
    r = run_bass_kernel_spmd(nc, [{f"in_{n}": a for n, a in arrays.items()}], core_ids=[0])
    y = np.asarray(r.results[0]["out_y"])
    return np.ascontiguousarray(y.transpose(1, 3, 0, 2).reshape(BATCH, OUT))
```

```python
from contextlib import ExitStack

import concourse.bass as bass
import numpy as np
from concourse import mybir

F32 = mybir.dt.float32
F32R = mybir.dt.float32r
ALU = mybir.AluOpType
ACT = mybir.ActivationFunctionType

BATCH, FIELDS, EMB, OUT = 2048, 32, 64, 256
PAIRS = FIELDS * (FIELDS - 1) // 2
COLS = 512
TILES = BATCH // COLS
QUADS = FIELDS // 4

MOVING_SLOTS = 12
TERM_RING = 3
PRODUCT_RING = 16
PAIR_RING = 4
GROUP = 4
WEIGHT_RING = 4
RAW_RING = 4
SUM_GROUP = 4
SUM_LAG = 3
UNFOLDED = (28,)
PER_BANK = 32


def plan_units():
    units = []

    def quads(v):
        for u in range(v):
            units.extend([("quad", u, 4 * v + t) for t in range(4)])

    quads(4)
    quads(3)
    units += [("ab", 4, None), ("ab", 3, None), ("cc", 4, 3), ("ab", 5, None)]
    quads(5)
    quads(2)
    units += [("ab", 2, None), ("cc", 5, 2), ("ab", 6, None), ("ab", 0, None)]
    quads(6)
    quads(1)
    units += [("ab", 1, None), ("cc", 6, 1), ("ab", 7, None), ("cc", 0, 7)]
    quads(7)
    return units


UNITS = plan_units()
N = len(UNITS)
GROUPS = N // GROUP
SUM_GROUPS = N // SUM_GROUP
BANKS = -(-N // PER_BANK)

MOVING_FIELDS = [(16, 8, 4), (17, 9, 5), (18, 10, 6), (19, 11, 7), (12, 24, 28), (13, 25), (14, 26),
                 (15, 27), (20, 2), (21, 1, 29), (22, 30), (23, 3, 31)]
PAIR_QUADS = [4, 3, 5, 2, 6, 0, 1, 7]

TERM_SLOT = [n % 3 if n < 16 else -n % 3 if n < 24 else (n + 2) % 3 for n in range(N)]
PRODUCT_SLOT = [n % PRODUCT_RING for n in range(N)]
WEIGHT_SLOT = [g % WEIGHT_RING for g in range(GROUPS)]


def free_after(slots, n):
    before = [m for m in range(len(slots)) if slots[m] == slots[n] and m < n]
    return before[-1] + 1 if before else max(m for m in range(len(slots)) if slots[m] == slots[n]) + 1 - len(slots)


def sums_after(n):
    g = n // SUM_GROUP
    if n % SUM_GROUP < SUM_GROUP - 1 or g == SUM_LAG - 1:
        return []
    if g < SUM_LAG:
        return [(1, SUM_GROUPS - 2 + g)]
    return [(0, g - SUM_LAG)] + ([(0, g - SUM_LAG + 1)] if g == SUM_GROUPS - 1 else [])


def chunk_fields(unit, c):
    kind, v, w = unit
    if kind == "quad":
        return (w,)
    if kind == "ab":
        return ((4 * v + 3,), (4 * v + 1, 4 * v + 3))[c]
    return (4 * (v, w)[c] + 2,)


def fields_of(unit):
    return chunk_fields(unit, 0) + chunk_fields(unit, 1)


FIRST_USE = {j: min(n for n in range(N) if j in fields_of(UNITS[n])) for j in range(1, FIELDS)}
LAST_USE = {j: max(n for n in range(N) if j in fields_of(UNITS[n])) for j in range(1, FIELDS)}
QUAD_USES = [[n for n in range(N) if UNITS[n][:2] == ("quad", u)] for u in range(QUADS - 1)]
PAIR_USES = [[n for n in range(N) if UNITS[n][0] != "quad" and v in UNITS[n][1:]] for v in PAIR_QUADS]


def pair_index(i, j):
    return i * (FIELDS - 1) - i * (i - 1) // 2 + j - i - 1


def unit_pairs(unit):
    kind, v, w = unit
    if kind == "quad":
        return [(4 * v + t, w) for t in range(4)]
    if kind == "ab":
        return [(4 * v, 4 * v + 3), (4 * v + 1, 4 * v + 3), (4 * v + 2, 4 * v + 3), (4 * v, 4 * v + 1)]
    return [(4 * q + t, 4 * q + 2) for q in (v, w) for t in range(2)]


def chunk_columns(unit, c):
    pairs = [pair_index(i, j) for i, j in unit_pairs(unit)]
    if unit[0] == "quad":
        return [(pair, 32 * c + e) for pair in pairs for e in range(32)]
    return [(pair, e) for pair in pairs[2 * c:2 * c + 2] for e in range(EMB)]


SEL_WIDTH = 60


def selectors():
    sel = np.zeros((128, 3, SEL_WIDTH), np.float32)
    for t in range(4):
        sel[32 * t:32 * t + 32, 0, 28 + t] = 1
    for t in range(2):
        sel[64 * t:64 * t + 64, 1, 28 + t] = 1
        sel[64 * t:64 * t + 64, 2, 30 + t] = 1
    return sel


def row_of(n):
    return n // PER_BANK, n % 4, 4 * (n % PER_BANK // 4)


def pair_slots():
    slots = np.full((BANKS, 128), -1)
    for n, unit in enumerate(UNITS):
        k, q, r = row_of(n)
        slots[k, 32 * q + r:32 * q + r + 4] = [pair_index(i, j) for i, j in unit_pairs(unit)]
    return slots


LOADS = sorted(range(FIELDS // 2), key=lambda p: min(FIRST_USE[j] for j in (2 * p, 2 * p + 1) if j))
MADE = [j for p in LOADS for j in (2 * p, 2 * p + 1) if j]
RANK = {j: n for n, j in enumerate(MADE)}


def fields_in(p):
    return [j for j in (2 * p, 2 * p + 1) if j]


def moving_slot(j):
    return next(s for s, fields in enumerate(MOVING_FIELDS) if j in fields)


def slot_free(j):
    fields = MOVING_FIELDS[moving_slot(j)]
    at = fields.index(j)
    return LAST_USE[fields[at - 1]] + 1 - (0 if at else N)


CUT = N - 16
LEAD = 12
SPACING = 2
FIRST_DELAY = 4
DUE = {}
for j in reversed(MADE):
    needed = min(FIRST_USE[i] for i in fields_in(j // 2)) - LEAD
    DUE[j] = min([needed] + [DUE[i] - SPACING for i in MADE[RANK[j] + 1:RANK[j] + 2]])
for j in MADE:
    DUE[j] = max([slot_free(j), DUE[j], -LEAD] + [DUE[i] for i in MADE[:RANK[j]]])


def due_of(j, first):
    return DUE[j] + (FIRST_DELAY if first and 0 <= DUE[j] < 8 else 0)


def in_window(due):
    return (due, 0) if due < CUT else (due - N, 1)


QUAD_GROUPS = [g for g in range(SUM_GROUPS) if UNITS[SUM_GROUP * g][0] == "quad"]
FOLDED = [g for g in QUAD_GROUPS if g not in UNFOLDED]
FOLDED_FIRST = [g for g in FOLDED if g >= 25 or g % 2 or g in (16, 20)]


def low_by_vector(j):
    return j // 2 in (3, 7, 11)


def split_by_vector(g):
    return g < 3 or g % 4 == 0


def bass_pair_interactions(nc, x, x_quads, x_pairs, k, wt, bias, sel, out):
    with ExitStack() as ctx:
        def sb(name, shape, dt=F32):
            return ctx.enter_context(nc.sbuf_tensor(name, shape, dt))

        def sem(name):
            return ctx.enter_context(nc.semaphore(name))

        weights = sb("weights", [128, WEIGHT_RING, GROUP * 256], F32R)
        raw_k = sb("raw_k", [128, RAW_RING, GROUP * 256])
        raw_x = sb("raw_x", [128, 2, 2, COLS])
        moving = sb("moving", [128, MOVING_SLOTS, 2, COLS], F32R)
        quad_x = sb("quad_x", [128, QUADS - 1, 2, COLS])
        pair_x = sb("pair_x", [128, PAIR_RING, 2, COLS])
        products = sb("products", [128, PRODUCT_RING, 2, COLS])
        pair_sums = sb("pair_sums", [128, BANKS, COLS])
        wt_sb = raw_k[:, RAW_RING - 1, :].rearrange("p (k o) -> p k o", k=BANKS)
        bias_sb = sb("bias_sb", [128, 2])
        sel_sb = sb("sel_sb", [128, 3, SEL_WIDTH])
        y_sb = sb("y_sb", [128, COLS])
        split_k = nc.dram_tensor("split_k", [GROUPS, 128, GROUP * 256], F32).ap()

        terms = [ctx.enter_context(nc.psum_tensor(f"terms{i}", [128, 2, COLS], F32)) for i in range(TERM_RING)]
        sums = ctx.enter_context(nc.psum_tensor("sums", [128, COLS], F32))
        y_ps = ctx.enter_context(nc.psum_tensor("y_ps", [128, COLS], F32))

        consts_landed = sem("consts_landed")
        w_landed = sem("w_landed")
        raw_k_landed = [sem(f"raw_k_landed{i}") for i in range(RAW_RING)]
        raw_x_landed = [sem(f"raw_x_landed{i}") for i in range(2)]
        weights_landed = [sem(f"weights_landed{i}") for i in range(WEIGHT_RING)]
        split_stored = [sem(f"split_stored{i}") for i in range(WEIGHT_RING)]
        quad_x_landed = [sem(f"quad_x_landed{i}") for i in range(QUADS - 1)]
        pair_x_landed = [sem(f"pair_x_landed{i}") for i in range(PAIR_RING)]
        weights_rounded = sem("weights_rounded")
        weights_split = sem("weights_split")
        weights_split_dve = sem("weights_split_dve")
        highs_ready = sem("highs_ready")
        lows_ready = sem("lows_ready")
        lows_ready_dve = sem("lows_ready_dve")
        terms_ready = sem("terms_ready")
        products_ready = sem("products_ready")
        folds_ready = sem("folds_ready")
        groups_summed = sem("groups_summed")
        sums_saved = sem("sums_saved")
        y_ready = sem("y_ready")
        y_saved = sem("y_saved")
        y_stored = sem("y_stored")

        def wait(eng, s, tile, per_tile, more):
            if isinstance(tile, int):
                if per_tile * tile + more > 0:
                    eng.wait_ge(s, per_tile * tile + more)
            else:
                eng.wait_ge(s, tile * per_tile + more)

        def wait_split(eng, g):
            mine = sum(split_by_vector(f) == split_by_vector(g) for f in range(g + 1))
            eng.wait_ge(weights_split_dve if split_by_vector(g) else weights_split, mine)

        def wait_lows(eng, tile, fields):
            for s in (lows_ready, lows_ready_dve):
                mine = [j for j in MADE if low_by_vector(j) == (s is lows_ready_dve)]
                last = [mine.index(j) for j in fields if j in mine]
                if last:
                    wait(eng, s, tile, len(mine), max(last) + 1)

        def wait_folded(eng, tile, g):
            if isinstance(tile, int) and tile == 0:
                eng.wait_ge(folds_ready, FOLDED_FIRST.index(g) + 1)
            else:
                wait(eng, folds_ready, tile, len(FOLDED), len(FOLDED_FIRST) - len(FOLDED) + FOLDED.index(g) + 1)

        def each_tile(eng, one_tile):
            one_tile(0, True)
            with eng.Fori(1, TILES) as tile:
                one_tile(tile, False)

        def low_operands(j):
            at = moving_slot(j)
            return (moving[:, at, 1, :], raw_x[:, LOADS.index(j // 2) % 2, j % 2, :], moving[:, at, 0, :].bitcast(F32))

        def low_k_operands(g):
            w = weights[:, g % WEIGHT_RING, :]
            return w[EMB:2 * EMB], raw_k[0:EMB, g % RAW_RING, :], w[0:EMB].bitcast(F32)

        block = ctx.enter_context(nc.Block())

        @block.sync
        def _(sp):
            def one_tile(tile, first):
                todo = []
                for g in range(GROUPS):
                    raw_due = {0: -N, 1: -9, 2: -8, 3: -7}.get(g, GROUP * (g - 5) + 2)
                    todo.append((raw_due if first else GROUP * free_after(WEIGHT_SLOT, g), 2, "k", g))
                for n, p in enumerate(LOADS):
                    if first and n < 2:
                        due = (-N + 1, -10)[n]
                    else:
                        due = max(DUE[max(1, 2 * p)] - 4, DUE[fields_in(LOADS[n - 2])[-1]] - (0 if n > 1 else N))
                    todo.append((due, 4, "x", n))
                for u in range(QUADS - 1):
                    todo.append((QUAD_USES[u][0] - (12 if u else 16) if first else QUAD_USES[u][-1] + 1 - N, 1, "quad", u))
                for a in range(QUADS):
                    todo.append((PAIR_USES[a][0] - 16, 1, "pair", a))
                for _, _, kind, a in sorted(todo):
                    if kind == "k" and first:
                        if a >= RAW_RING:
                            wait_split(sp, a - RAW_RING)
                        sp.dma_start(raw_k[0:EMB, a % RAW_RING, :], k[a]).then_inc(raw_k_landed[a % RAW_RING], 16)
                    elif kind == "k":
                        sp.wait_ge(split_stored[a % WEIGHT_RING], 16 * WEIGHT_SLOT.count(a % WEIGHT_RING))
                        wait(sp, terms_ready, tile, N, GROUP * free_after(WEIGHT_SLOT, a))
                        sp.dma_start(weights[:, a % WEIGHT_RING, :].bitcast(F32), split_k[a]).then_inc(weights_landed[a % WEIGHT_RING], 16)
                    elif kind == "x":
                        at = (tile * FIELDS + 2 * LOADS[a]) * EMB * COLS
                        source = x[at:at + 2 * EMB * COLS] if first else x[bass.ds(sp.snap(at), 2 * EMB * COLS)]
                        if a > 1:
                            wait_lows(sp, tile, fields_in(LOADS[a - 2]))
                        else:
                            wait(sp, terms_ready, tile, N, max(FIRST_USE[j] for j in fields_in(LOADS[a - 2])) + 1 - N)
                        for h in range(2):
                            sp.dma_start(raw_x[64 * h:64 * h + 64, a % 2], source.rearrange("(f e b) -> e f b", f=2, b=COLS)
                                         ).then_inc(raw_x_landed[a % 2], 16)
                    elif kind == "quad":
                        wait(sp, products_ready, tile, N, QUAD_USES[a][-1] + 1 - N)
                        sp.dma_start(quad_x[:, a], x_quads[tile, a]).then_inc(quad_x_landed[a], 16)
                    else:
                        at = (tile * QUADS + PAIR_QUADS[a]) * 256 * COLS
                        source = x_pairs[at:at + 256 * COLS] if first else x_pairs[bass.ds(sp.snap(at), 256 * COLS)]
                        wait(sp, products_ready, tile, N, PAIR_USES[a - PAIR_RING][-1] + 1 - (0 if a >= PAIR_RING else N))
                        sp.dma_start(pair_x[:, a % PAIR_RING], source.rearrange("(p m b) -> p m b", m=2, b=COLS)
                                     ).then_inc(pair_x_landed[a % PAIR_RING], 16)

            def load_w():
                wait_split(sp, max(g for g in range(GROUPS) if g % RAW_RING == RAW_RING - 1))
                sp.dma_start(wt_sb, wt).then_inc(w_landed, 16)

            one_tile(0, True)
            load_w()
            with sp.Fori(1, TILES) as tile:
                one_tile(tile, False)

        @block.tensor
        def _(pe):
            def sum_group(tile, g, folded=True):
                if isinstance(tile, int) and tile == 0 and g == 0:
                    pe.wait_ge(consts_landed, 32)
                group = range(SUM_GROUP * g, SUM_GROUP * (g + 1))
                if SUM_GROUP * g % PER_BANK == 0:
                    wait(pe, sums_saved, tile, BANKS, SUM_GROUP * g // PER_BANK)
                if folded and g in (FOLDED_FIRST if isinstance(tile, int) and tile == 0 else FOLDED):
                    wait_folded(pe, tile, g)
                    chunks = [0]
                else:
                    wait(pe, products_ready, tile, N, SUM_GROUP * (g + 1))
                    chunks = [0, 1]
                for c in chunks:
                    for n in group:
                        _, q, r = row_of(n)
                        s = 0 if UNITS[n][0] == "quad" else 1 + c
                        last = pe.matmul(sums[32 * q:32 * q + 32, :], sel_sb[:, s, 28 - r:60 - r],
                                         products[:, PRODUCT_SLOT[n], c, :], start=c == 0 and n % PER_BANK < 4,
                                         stop=False, tile_position=(0, 32 * q), skip_group_check=True)
                last.then_inc(groups_summed, 1)

            def y_part(h, k, to):
                return pe.matmul(to, wt_sb[:, k, 128 * h:128 * h + 128], pair_sums[:, k, :], start=k == 0, stop=k == BANKS - 1)

            def one_tile(tile, first):
                for n, unit in enumerate(UNITS):
                    if n % GROUP == 0:
                        g = n // GROUP
                        if first:
                            wait_split(pe, g)
                        else:
                            per = WEIGHT_SLOT.count(g % WEIGHT_RING)
                            wait(pe, weights_landed[g % WEIGHT_RING], tile, 16 * per, 16 * (g // WEIGHT_RING + 1 - per))
                    new = [j for j in FIRST_USE if FIRST_USE[j] == n]
                    wait_lows(pe, tile, new)
                    wait(pe, products_ready, tile, N, free_after(TERM_SLOT, n))
                    for c in range(2):
                        at = 256 * (n % GROUP) + 128 * c
                        for j, rows in zip(chunk_fields(unit, c), (128, 64)):
                            for part in range(2):
                                mm = pe.matmul(terms[TERM_SLOT[n]][0:rows, c, :], weights[:, n // GROUP % WEIGHT_RING, at:at + rows],
                                               moving[:, moving_slot(j), part, :], start=part == 0, stop=part == 1)
                    mm.then_inc(terms_ready, 1)
                    for back, g in sums_after(n):
                        if not (first and back):
                            sum_group(tile - back, g)
                    if not first and n in Y_AT:
                        h, k = Y_AT[n]
                        if (h, k) == (0, 0):
                            wait(pe, sums_saved, tile, BANKS, 0)
                            pe.wait_ge(w_landed, 16)
                        if (h, k) == (1, 0):
                            wait(pe, y_saved, tile, 2, -1)
                        mm = y_part(h, k, y_ps[:, :])
                        if k == BANKS - 1:
                            mm.then_inc(y_ready, 1)

            each_tile(pe, one_tile)
            sum_group(TILES - 1, SUM_GROUPS - 2)
            sum_group(TILES - 1, SUM_GROUPS - 1, folded=False)
            pe.wait_ge(y_saved, 2 * (TILES - 1))
            last_y = (y_ps[:, :], terms[0][:, 0, :])
            for k in range(BANKS):
                if k == BANKS - 1:
                    pe.wait_ge(sums_saved, BANKS * TILES)
                for h in range(2):
                    mm = y_part(h, k, last_y[h])
                    if k == BANKS - 1:
                        mm.then_inc(y_ready, 1)

        @block.vector
        def _(dve):
            def low_k(g):
                dve.wait_ge(weights_rounded, g + 1)
                nc.vector.tensor_tensor(*low_k_operands(g), ALU.subtract).then_inc(weights_split_dve, 1)

            def one_tile(tile, first):
                for n, (kind, u, w) in enumerate(UNITS):
                    for j in MADE:
                        if low_by_vector(j) and due_of(j, first) + 2 == n:
                            wait(dve, highs_ready, tile, len(MADE), RANK[j] + 1)
                            nc.vector.tensor_tensor(*low_operands(j), ALU.subtract).then_inc(lows_ready_dve, 1)
                    for g in range(GROUPS):
                        if first and split_by_vector(g) and n == max(0, g, GROUP * (g - 3) + 2):
                            low_k(g)
                    if kind == "quad" and n == QUAD_USES[u][0]:
                        wait(dve, quad_x_landed[u], tile, 16, 16)
                    for a, v in enumerate(PAIR_QUADS):
                        if PAIR_USES[a][0] == n:
                            per = QUADS // PAIR_RING
                            wait(dve, pair_x_landed[a % PAIR_RING], tile, 16 * per, 16 * (a // PAIR_RING + 1))
                    wait(dve, groups_summed, tile, SUM_GROUPS, -(-free_after(PRODUCT_SLOT, n) // SUM_GROUP))
                    wait(dve, terms_ready, tile, N, n + 1)
                    if kind == "quad":
                        xi = quad_x[:, u]
                    elif kind == "ab":
                        xi = pair_x[:, PAIR_QUADS.index(u) % PAIR_RING]
                    else:
                        lo, hi = sorted(PAIR_QUADS.index(v) % PAIR_RING for v in (u, w))
                        xi = pair_x[:, lo:hi + 1:hi - lo, 0, :]
                    nc.vector.tensor_tensor(products[:, PRODUCT_SLOT[n]], terms[TERM_SLOT[n]][:, :, :], xi,
                                            ALU.mult).then_inc(products_ready, 1)

            each_tile(dve, one_tile)

        @block.gpsimd
        def _(pool):
            def low(tile, j):
                wait(pool, highs_ready, tile, len(MADE), RANK[j] + 1)
                nc.gpsimd.tensor_tensor(*low_operands(j), ALU.subtract).then_inc(lows_ready, 1)

            def low_k(g, lows, folds):
                wait(pool, lows_ready, 0, 0, lows)
                wait(pool, folds_ready, 0, 0, folds)
                pool.wait_ge(weights_rounded, g + 1)
                nc.gpsimd.tensor_tensor(*low_k_operands(g), ALU.subtract).then_inc(weights_split, 1)
                wait_split(pool, g)

            def fold(tile, g):
                wait(pool, products_ready, tile, N, SUM_GROUP * (g + 1))
                at = PRODUCT_SLOT[SUM_GROUP * g]
                z = products[:, at:at + SUM_GROUP]
                nc.gpsimd.tensor_tensor(z[:, :, 0, :], z[:, :, 0, :], z[:, :, 1, :], ALU.add).then_inc(folds_ready, 1)

            def one_tile(tile, first):
                todo = [(*in_window(due_of(j, first)), "low", RANK[j]) for j in MADE if not low_by_vector(j)]
                todo += [(*in_window(SUM_GROUP * (g + 1) + 1), "fold", g) for g in (FOLDED_FIRST if first else FOLDED)]
                if first:
                    todo += [(GROUP * (g - 3) + 1, 0, "low_k", g) for g in range(GROUPS) if not split_by_vector(g)]
                lows = folds = 0
                for _, back, kind, a in sorted(todo):
                    if kind == "low_k":
                        low_k(a, lows, folds)
                    elif kind == "low":
                        low(tile, MADE[a])
                        lows += 1
                    elif not (first and back):
                        fold(tile - back, a)
                        folds += 1

            each_tile(pool, one_tile)
            for g in FOLDED:
                if in_window(SUM_GROUP * (g + 1) + 1)[1] and g < SUM_GROUPS - 1:
                    fold(TILES - 1, g)

        @block.scalar
        def _(act):
            def high(tile, j):
                at = LOADS.index(j // 2)
                per = len(LOADS) // 2
                wait(act, raw_x_landed[at % 2], tile, 32 * per, 32 * (at // 2 + 1))
                wait(act, terms_ready, tile, N, slot_free(j))
                nc.scalar.copy(moving[:, moving_slot(j), 0, :], raw_x[:, at % 2, j % 2, :]).then_inc(highs_ready, 1)

            def round_k(g):
                act.wait_ge(raw_k_landed[g % RAW_RING], 16 * (g // RAW_RING + 1))
                if g >= WEIGHT_RING:
                    act.wait_ge(terms_ready, GROUP * (g - WEIGHT_RING + 1))
                    act.wait_ge(split_stored[g % WEIGHT_RING], 16 * (g // WEIGHT_RING))
                nc.scalar.copy(weights[0:EMB, g % WEIGHT_RING, :], raw_k[0:EMB, g % RAW_RING, :]).then_inc(weights_rounded, 1)

            def save_sums(tile, k):
                wait(act, groups_summed, tile, SUM_GROUPS, min((k + 1) * PER_BANK // SUM_GROUP, SUM_GROUPS))
                nc.scalar.copy(pair_sums[:, k, :], sums[:, :]).then_inc(sums_saved, 1)

            def save_y(tile, h, source=y_ps[:, :], to=y_sb[:, :]):
                wait(act, y_ready, tile, 2, h + 1)
                nc.scalar.activation(to, source, ACT.Identity, bias=bias_sb[:, h:h + 1]).then_inc(y_saved, 1)
                wait(act, y_saved, tile, 2, h + 1)
                act.dma_start(out[h, tile], to).then_inc(y_stored, 16)

            def y_sb_free(tile, h):
                wait(act, y_stored, tile, 32, 16 * (h + 1))

            def one_tile(tile, first):
                todo = [(*in_window(due_of(j, first) - 1), "high", RANK[j]) for j in MADE]
                todo += [(*in_window(min(PER_BANK * (k + 1) + SUM_GROUP * SUM_LAG - 1, N + SUM_GROUP * 2)), "sums", k) for k in range(BANKS)]
                y_at = [max(n for n in Y_AT if Y_AT[n][0] == h) + 1 for h in range(2)]
                todo += [(y_at[h], 1, "y", h) for h in range(2)] + [(y_at[h] + 7, 1, "y_sb_free", h) for h in range(2)]
                if first:
                    todo += [(GROUP * (g - 3) if g else -N, 0, "round_k", g) for g in range(GROUPS)]
                    todo += [(GROUP * (g - 3) + (4 if split_by_vector(g) else 6), 0, "store_k", g) for g in range(GROUPS)]
                    todo += [(0, 0, "consts", a) for a in range(2)]
                for _, back, kind, a in sorted(todo):
                    if kind == "high":
                        high(tile, MADE[a])
                    elif kind == "round_k":
                        round_k(a)
                    elif kind == "store_k":
                        wait_split(act, a)
                        act.dma_start(split_k[a], weights[:, a % WEIGHT_RING, :].bitcast(F32)).then_inc(split_stored[a % WEIGHT_RING], 16)
                    elif kind == "consts":
                        chip, dram = ((sel_sb, sel), (bias_sb, bias))[a]
                        act.dma_start(chip[:], dram).then_inc(consts_landed, 16)
                    elif not (first and back):
                        {"sums": save_sums, "y": save_y, "y_sb_free": y_sb_free}[kind](tile - back, a)

            each_tile(act, one_tile)
            save_sums(TILES - 1, BANKS - 1)
            save_y(TILES - 1, 0)
            save_y(TILES - 1, 1, terms[0][:, 0, :], products[:, 0, 0, :])
            act.wait_ge(y_stored, 32 * TILES)


Y_AT = {13: (0, 0), 17: (0, 1), 21: (0, 2), 29: (0, 3), 37: (1, 0), 49: (1, 1), 61: (1, 2), 73: (1, 3)}


def kernel(r_feat_emb, L0_rec_kernel, L0_rec_W, L0_rec_b):
    import concourse.bacc as bacc
    from concourse.bass_utils import run_bass_kernel_spmd

    x = np.ascontiguousarray(np.asarray(r_feat_emb).reshape(TILES, COLS, FIELDS, EMB).transpose(0, 2, 3, 1))
    x_quads = x.reshape(TILES, QUADS, 4, 2, 32, COLS)[:, :QUADS - 1].transpose(0, 1, 2, 4, 3, 5)
    x_quads = np.ascontiguousarray(x_quads.reshape(TILES, QUADS - 1, 128, 2, COLS))
    x_pairs = x.reshape(TILES, QUADS, 4, EMB, COLS)[:, :, [0, 2, 1, 0]].reshape(TILES, QUADS, 2, 2, EMB, COLS)
    x_pairs = np.ascontiguousarray(x_pairs.transpose(0, 1, 2, 4, 3, 5)).reshape(-1)
    cols = [col for unit in UNITS for c in range(2) for col in chunk_columns(unit, c)]
    k = np.asarray(L0_rec_kernel).reshape(EMB, PAIRS * EMB)[:, [pair * EMB + e for pair, e in cols]]
    k = np.ascontiguousarray(k.reshape(EMB, GROUPS, -1).transpose(1, 0, 2))
    slots = pair_slots().T
    w = np.asarray(L0_rec_W)
    wt = np.zeros((128, BANKS, OUT), w.dtype)
    wt[slots >= 0] = w.T[slots[slots >= 0]]
    bias = np.ascontiguousarray(np.asarray(L0_rec_b).reshape(2, 128).T)
    arrays = {"x": x.reshape(-1), "x_quads": x_quads, "x_pairs": x_pairs, "k": k, "wt": wt, "bias": bias, "sel": selectors()}

    nc = bacc.Bacc("TRN2", target_bir_lowering=False, num_devices=1)
    args = [nc.dram_tensor(f"in_{n}", a.shape, mybir.dt.from_np(a.dtype), kind="ExternalInput").ap()
            for n, a in arrays.items()]
    out = nc.dram_tensor("out_y", [2, TILES, 128, COLS], F32, kind="ExternalOutput").ap()
    bass_pair_interactions(nc, *args, out)
    r = run_bass_kernel_spmd(nc, [{f"in_{n}": a for n, a in arrays.items()}], core_ids=[0])
    y = np.asarray(r.results[0]["out_y"])
    return np.ascontiguousarray(y.transpose(1, 3, 0, 2).reshape(BATCH, OUT))
```
